# Optimizing a Trainium2 kernel written in Bass

```python
import numpy as np
import jax
import jax.numpy as jnp

def _softmax(x, axis=-1):
    return jax.nn.softmax(x, axis=axis)

def _gelu(x):
    return jax.nn.gelu(x, approximate=True)

def _silu(x):
    return jax.nn.silu(x)

def _sigmoid(x):
    return jax.nn.sigmoid(x)

def _layernorm(x, axis=-1, eps=1e-05):
    m = jnp.mean(x, axis=axis, keepdims=True)
    v = jnp.var(x, axis=axis, keepdims=True)
    return (x - m) / jnp.sqrt(v + eps)

def _scatter_add(tgt, idx, src, axis=0):
    return tgt.at[idx].add(src)

def _segment_sum(src, seg, n):
    return jax.ops.segment_sum(src, seg, n)
kernel_name = 'mk_xattn_seq_d2_seqx_r4_fa158f'

def setup_inputs(seed: int=0):
    np.random.seed(seed)
    _w = jnp.asarray

    def _rec_inputs():
        import jax
        import jax.numpy as jnp
        _rk = jax.random.key(seed)
        x = -0.0002928 + 1 * jax.random.normal(jax.random.fold_in(_rk, 1), (64, 256, 256), jnp.float32)
        _lenS = 256 - jax.random.randint(jax.random.fold_in(_rk, 7), (64,), 0, max(1, 256 // 4) + 1, jnp.int32)
        _lenS2 = 77 - jax.random.randint(jax.random.fold_in(_rk, 8), (64,), 0, max(1, 77 // 4) + 1, jnp.int32)
        _ctx_1024P = jax.random.normal(jax.random.fold_in(_rk, 11), (64, 16, 256), jnp.float32)
        _ctx_1024c = jax.random.dirichlet(jax.random.fold_in(_rk, 511), 0.3 * jnp.ones((16,), jnp.float32), (64, 77))
        _ctx_1024t = jnp.einsum('bsk,bkd->bsd', _ctx_1024c, _ctx_1024P)
        _ctx_1024t = _ctx_1024t * jax.lax.rsqrt(jnp.mean(jnp.square(_ctx_1024t)) + 1e-12) * 0.953939
        ctx_1024 = -1.39393e-06 + 0.999914 * (_ctx_1024t + 0.3 * jax.random.normal(jax.random.fold_in(_rk, 611), (64, 77, 256), jnp.float32))
        return (x, ctx_1024)
    x, ctx_1024 = _rec_inputs()

    def _L0_xattn_setup():
        import jax, jax.numpy as jnp
        import numpy as np
        B, Q, KV = (2, 512, 512)
        D_MODEL = 256
        N_HEADS = 16
        D_KV = 64
        EPS = 1e-06
        key = jax.random.key(seed)
        ks = jax.random.split(key, 7)
        s = 0.02
        return {'hidden_states': jax.random.normal(ks[0], (B, Q, D_MODEL), jnp.float32), 'key_value_states': jax.random.normal(ks[1], (B, KV, D_MODEL), jnp.float32), 'wq': jax.random.normal(ks[2], (D_MODEL, N_HEADS * D_KV), jnp.float32) * s, 'wk': jax.random.normal(ks[3], (D_MODEL, N_HEADS * D_KV), jnp.float32) * s, 'wv': jax.random.normal(ks[4], (D_MODEL, N_HEADS * D_KV), jnp.float32) * s, 'wo': jax.random.normal(ks[5], (N_HEADS * D_KV, D_MODEL), jnp.float32) * s, 'norm_w': jnp.ones((D_MODEL,), jnp.float32)}
    _L0_xattn_all = _L0_xattn_setup()
    _L0_xattn_in = {k: v for k, v in _L0_xattn_all.items() if k in ('wq', 'wk', 'wv', 'wo', 'norm_w')}
    del _L0_xattn_all

    def _L1_xattn_setup():
        import jax, jax.numpy as jnp
        import numpy as np
        B, T, SE, C, H = (2, 512, 512, 256, 16)
        HS = C // H
        EPS = 1e-05

        def _ln(x, g, b):
            mu = jnp.mean(x, axis=-1, keepdims=True)
            var = jnp.mean(jnp.square(x - mu), axis=-1, keepdims=True)
            return (x - mu) * jax.lax.rsqrt(var + EPS) * g + b

        def _mha(q_in, kv_in, wq, bq, wk, bk, wv, bv, causal):
            q = jnp.einsum('btc,hcd->bhtd', q_in, wq) + bq[None, :, None, :]
            k = jnp.einsum('bsc,hcd->bhsd', kv_in, wk) + bk[None, :, None, :]
            v = jnp.einsum('bsc,hcd->bhsd', kv_in, wv) + bv[None, :, None, :]
            scores = jnp.einsum('bhtd,bhsd->bhts', q, k) * q.shape[-1] ** (-0.5)
            if causal:
                t, s = (scores.shape[-2], scores.shape[-1])
                mask = jnp.tril(jnp.ones((t, s), bool))
                scores = jnp.where(mask, scores, -jnp.inf)
            p = jax.nn.softmax(scores, axis=-1)
            o = jnp.einsum('bhts,bhsd->bhtd', p, v)
            b_, h_, t_, d_ = o.shape
            return o.transpose(0, 2, 1, 3).reshape(b_, t_, h_ * d_)
        key = jax.random.key(seed)
        ks = iter(jax.random.split(key, 40))
        nrm = lambda shape, s=0.02: jax.random.normal(next(ks), shape, jnp.float32) * s
        inp = {'x_e': jax.random.normal(next(ks), (B, SE, C), jnp.float32), 'x': jax.random.normal(next(ks), (B, T, C), jnp.float32), 'mq_w': nrm((H, C, HS)), 'mq_b': nrm((H, HS)), 'mk_w': nrm((H, C, HS)), 'mk_b': nrm((H, HS)), 'mv_w': nrm((H, C, HS)), 'mv_b': nrm((H, HS)), 'm_proj_w': nrm((C, C)), 'm_proj_b': nrm((C,)), 'cq_w': nrm((H, C, HS)), 'cq_b': nrm((H, HS)), 'ck_w': nrm((H, C, HS)), 'ck_b': nrm((H, HS)), 'cv_w': nrm((H, C, HS)), 'cv_b': nrm((H, HS)), 'c_proj_w': nrm((C, C)), 'c_proj_b': nrm((C,)), 'f_w1': nrm((C, 4 * C)), 'f_b1': nrm((4 * C,)), 'f_w2': nrm((4 * C, C)), 'f_b2': nrm((C,)), 'ln1_g': jnp.ones((C,), jnp.float32), 'ln1_b': jnp.zeros((C,), jnp.float32), 'ln2_g': jnp.ones((C,), jnp.float32), 'ln2_b': jnp.zeros((C,), jnp.float32), 'ln3_g': jnp.ones((C,), jnp.float32), 'ln3_b': jnp.zeros((C,), jnp.float32)}
        return inp
    _L1_xattn_all = _L1_xattn_setup()
    _L1_xattn_in = {k: v for k, v in _L1_xattn_all.items() if k in ('mq_w', 'mq_b', 'mk_w', 'mk_b', 'mv_w', 'mv_b', 'm_proj_w', 'm_proj_b', 'cq_w', 'cq_b', 'ck_w', 'ck_b', 'cv_w', 'cv_b', 'c_proj_w', 'c_proj_b', 'f_w1', 'f_b1', 'f_w2', 'f_b2', 'ln1_g', 'ln1_b', 'ln2_g', 'ln2_b', 'ln3_g', 'ln3_b')}
    del _L1_xattn_all
    return {'x': x, 'ctx_1024': ctx_1024, 'L0_xattn_wq': _L0_xattn_in['wq'], 'L0_xattn_wk': _L0_xattn_in['wk'], 'L0_xattn_wv': _L0_xattn_in['wv'], 'L0_xattn_wo': _L0_xattn_in['wo'], 'L0_xattn_norm_w': _L0_xattn_in['norm_w'], 'L1_xattn_mq_w': _L1_xattn_in['mq_w'], 'L1_xattn_mq_b': _L1_xattn_in['mq_b'], 'L1_xattn_mk_w': _L1_xattn_in['mk_w'], 'L1_xattn_mk_b': _L1_xattn_in['mk_b'], 'L1_xattn_mv_w': _L1_xattn_in['mv_w'], 'L1_xattn_mv_b': _L1_xattn_in['mv_b'], 'L1_xattn_m_proj_w': _L1_xattn_in['m_proj_w'], 'L1_xattn_m_proj_b': _L1_xattn_in['m_proj_b'], 'L1_xattn_cq_w': _L1_xattn_in['cq_w'], 'L1_xattn_cq_b': _L1_xattn_in['cq_b'], 'L1_xattn_ck_w': _L1_xattn_in['ck_w'], 'L1_xattn_ck_b': _L1_xattn_in['ck_b'], 'L1_xattn_cv_w': _L1_xattn_in['cv_w'], 'L1_xattn_cv_b': _L1_xattn_in['cv_b'], 'L1_xattn_c_proj_w': _L1_xattn_in['c_proj_w'], 'L1_xattn_c_proj_b': _L1_xattn_in['c_proj_b'], 'L1_xattn_f_w1': _L1_xattn_in['f_w1'], 'L1_xattn_f_b1': _L1_xattn_in['f_b1'], 'L1_xattn_f_w2': _L1_xattn_in['f_w2'], 'L1_xattn_f_b2': _L1_xattn_in['f_b2'], 'L1_xattn_ln1_g': _L1_xattn_in['ln1_g'], 'L1_xattn_ln1_b': _L1_xattn_in['ln1_b'], 'L1_xattn_ln2_g': _L1_xattn_in['ln2_g'], 'L1_xattn_ln2_b': _L1_xattn_in['ln2_b'], 'L1_xattn_ln3_g': _L1_xattn_in['ln3_g'], 'L1_xattn_ln3_b': _L1_xattn_in['ln3_b']}

def reference(x, ctx_1024, L0_xattn_wq, L0_xattn_wk, L0_xattn_wv, L0_xattn_wo, L0_xattn_norm_w, L1_xattn_mq_w, L1_xattn_mq_b, L1_xattn_mk_w, L1_xattn_mk_b, L1_xattn_mv_w, L1_xattn_mv_b, L1_xattn_m_proj_w, L1_xattn_m_proj_b, L1_xattn_cq_w, L1_xattn_cq_b, L1_xattn_ck_w, L1_xattn_ck_b, L1_xattn_cv_w, L1_xattn_cv_b, L1_xattn_c_proj_w, L1_xattn_c_proj_b, L1_xattn_f_w1, L1_xattn_f_b1, L1_xattn_f_w2, L1_xattn_f_b2, L1_xattn_ln1_g, L1_xattn_ln1_b, L1_xattn_ln2_g, L1_xattn_ln2_b, L1_xattn_ln3_g, L1_xattn_ln3_b):
    import jax
    import jax.numpy as jnp

    def _L0_xattn_ref(hidden_states, key_value_states, wq, wk, wv, wo, norm_w):
        import jax, jax.numpy as jnp
        import numpy as np
        B, Q, KV = (2, 512, 512)
        D_MODEL = 256
        N_HEADS = 16
        D_KV = 64
        EPS = 1e-06
        var = jnp.mean(jnp.square(hidden_states), axis=-1, keepdims=True)
        normed = hidden_states * jax.lax.rsqrt(var + EPS) * norm_w
        b, q_len, _ = hidden_states.shape
        kv_len = key_value_states.shape[1]

        def split_heads(x):
            return x.reshape(b, -1, N_HEADS, D_KV).transpose(0, 2, 1, 3)
        q = split_heads(normed @ wq)
        k = split_heads(key_value_states @ wk)
        v = split_heads(key_value_states @ wv)
        scores = jnp.einsum('bhqd,bhkd->bhqk', q, k)
        attn = jax.nn.softmax(scores.astype(jnp.float32), axis=-1).astype(scores.dtype)
        ctx = jnp.einsum('bhqk,bhkd->bhqd', attn, v)
        ctx = ctx.transpose(0, 2, 1, 3).reshape(b, q_len, N_HEADS * D_KV)
        attn_out = ctx @ wo
        return hidden_states + attn_out

    def _L1_xattn_ref(x_e, x, mq_w, mq_b, mk_w, mk_b, mv_w, mv_b, m_proj_w, m_proj_b, cq_w, cq_b, ck_w, ck_b, cv_w, cv_b, c_proj_w, c_proj_b, f_w1, f_b1, f_w2, f_b2, ln1_g, ln1_b, ln2_g, ln2_b, ln3_g, ln3_b):
        import jax, jax.numpy as jnp
        import numpy as np
        B, T, SE, C, H = (2, 512, 512, 256, 16)
        HS = C // H
        EPS = 1e-05

        def _ln(x, g, b):
            mu = jnp.mean(x, axis=-1, keepdims=True)
            var = jnp.mean(jnp.square(x - mu), axis=-1, keepdims=True)
            return (x - mu) * jax.lax.rsqrt(var + EPS) * g + b

        def _mha(q_in, kv_in, wq, bq, wk, bk, wv, bv, causal):
            q = jnp.einsum('btc,hcd->bhtd', q_in, wq) + bq[None, :, None, :]
            k = jnp.einsum('bsc,hcd->bhsd', kv_in, wk) + bk[None, :, None, :]
            v = jnp.einsum('bsc,hcd->bhsd', kv_in, wv) + bv[None, :, None, :]
            scores = jnp.einsum('bhtd,bhsd->bhts', q, k) * q.shape[-1] ** (-0.5)
            if causal:
                t, s = (scores.shape[-2], scores.shape[-1])
                mask = jnp.tril(jnp.ones((t, s), bool))
                scores = jnp.where(mask, scores, -jnp.inf)
            p = jax.nn.softmax(scores, axis=-1)
            o = jnp.einsum('bhts,bhsd->bhtd', p, v)
            b_, h_, t_, d_ = o.shape
            return o.transpose(0, 2, 1, 3).reshape(b_, t_, h_ * d_)
        h = _mha(_ln(x, ln1_g, ln1_b), _ln(x, ln1_g, ln1_b), mq_w, mq_b, mk_w, mk_b, mv_w, mv_b, causal=True)
        x = x + h @ m_proj_w + m_proj_b
        h = _mha(_ln(x, ln2_g, ln2_b), x_e, cq_w, cq_b, ck_w, ck_b, cv_w, cv_b, causal=False)
        x = x + h @ c_proj_w + c_proj_b
        h = jax.nn.relu(_ln(x, ln3_g, ln3_b) @ f_w1 + f_b1) @ f_w2 + f_b2
        return x + h
    x = _L0_xattn_ref(x, ctx_1024, L0_xattn_wq, L0_xattn_wk, L0_xattn_wv, L0_xattn_wo, L0_xattn_norm_w)
    x = _L1_xattn_ref(ctx_1024, x, L1_xattn_mq_w, L1_xattn_mq_b, L1_xattn_mk_w, L1_xattn_mk_b, L1_xattn_mv_w, L1_xattn_mv_b, L1_xattn_m_proj_w, L1_xattn_m_proj_b, L1_xattn_cq_w, L1_xattn_cq_b, L1_xattn_ck_w, L1_xattn_ck_b, L1_xattn_cv_w, L1_xattn_cv_b, L1_xattn_c_proj_w, L1_xattn_c_proj_b, L1_xattn_f_w1, L1_xattn_f_b1, L1_xattn_f_w2, L1_xattn_f_b2, L1_xattn_ln1_g, L1_xattn_ln1_b, L1_xattn_ln2_g, L1_xattn_ln2_b, L1_xattn_ln3_g, L1_xattn_ln3_b)
    return x

_drawn_inputs = setup_inputs


def setup_inputs(seed=0):
    import zlib

    import numpy as np

    out = dict(_drawn_inputs(seed))
    spreads = {'L0_xattn_norm_w': (1.0, 0.6),
     'L1_xattn_ln1_g': (1.0, 0.6),
     'L1_xattn_ln1_b': (0.0, 0.771),
     'L1_xattn_ln2_g': (1.0, 0.6),
     'L1_xattn_ln2_b': (0.0, 0.8),
     'L1_xattn_ln3_g': (1.0, 0.6),
     'L1_xattn_ln3_b': (0.0, 0.574)}
    factors = {'L1_xattn_mq_w': 8.0,
     'L1_xattn_mq_b': 29.982,
     'L1_xattn_mk_w': 8.0,
     'L1_xattn_mk_b': 64.0,
     'L1_xattn_mv_b': 8.0,
     'L1_xattn_m_proj_b': 2.783,
     'L1_xattn_cq_w': 8.0,
     'L1_xattn_cq_b': 51.959,
     'L1_xattn_ck_w': 8.0,
     'L1_xattn_ck_b': 64.0,
     'L1_xattn_cv_b': 8.0,
     'L1_xattn_c_proj_b': 3.078,
     'L1_xattn_f_b1': 6.392,
     'L1_xattn_f_b2': 2.946}
    for name, (base, spread) in spreads.items():
        noise = np.random.default_rng([zlib.crc32(name.encode()), seed]).standard_normal(out[name].shape)
        drawn = base * np.exp(spread * noise) if base else spread * noise
        out[name] = jnp.asarray(drawn.astype(out[name].dtype))
    for name, factor in factors.items():
        out[name] = (out[name] * factor).astype(out[name].dtype)
    return out
```

```python
from contextlib import ExitStack

import concourse.bass as bass
from concourse import mybir

ALU = mybir.AluOpType
ACT = mybir.ActivationFunctionType
AX_X = mybir.AxisListType.X
F32 = mybir.dt.float32
F32R = mybir.dt.float32r
F16 = mybir.dt.float16
BF16 = mybir.dt.bfloat16

P = 128
EPS_RMS = 1e-6
EPS_LN = 1e-5
MASKED = -1e30

RINGS = {"bank": 8, "probs0": 2, "probs1": 2, "probsT0": 2, "probsT1": 4,
         "split": 1, "chain": 1, "vsplit": 1, "max": 1}

USES = {
    "stat": {"chain": 2}, "rms": {"chain": 3}, "norm": {}, "turn": {"bank": 1, "split": 1},
    "q0": {"bank": 1}, "k0": {"bank": 1}, "v0": {"bank": 1, "vsplit": 1},
    "ctx": {"bank": 1, "split": 1},
    "qk0": {"bank": 1, "max": 1, "probs0": 1}, "tr0": {"bank": 1, "probsT0": 1, "split": 1}, "pv0": {"bank": 1, "chain": 1},
    "ct0": {"bank": 1}, "wo": {"bank": 1},
    "ck": {"bank": 1}, "cv": {"bank": 1, "vsplit": 1},
    "q1": {"bank": 1}, "k1": {"bank": 1}, "v1": {"bank": 1, "vsplit": 1},
    "qkA": {"bank": 1, "max": 1, "probs1": 1}, "qkB": {"bank": 1, "max": 1, "probs1": 1}, "qkC": {"bank": 1, "max": 1},
    "trA": {"bank": 1, "probsT1": 1, "split": 1}, "trB": {"bank": 1, "probsT1": 1, "split": 1},
    "pv": {"bank": 1, "chain": 2}, "ct": {"bank": 1, "split": 1}, "proj": {"bank": 1},
    "qk2": {"bank": 1, "max": 1, "probs1": 1}, "tr2": {"bank": 1, "probsT1": 1, "split": 1},
    "h": {"bank": 1}, "f2": {"bank": 1},
}


def steps(text):
    return [(name, *map(int, numbers)) for name, *numbers in (word.split(".") for word in text.split())]


LOOP_ORDER = steps("""
    turn.1.0 turn.1.1 qk0.1.0 qk0.1.1 k1 q1.1 tr0.1.0 qkA.0.0 v1 trA.0.0 qkA.0.1 qkA.0.2 tr0.1.1 trA.0.1
    pv.1.0.0 trA.0.2 qk0.1.2 qkA.0.3 qk0.1.3 qkB.1.0 qkC.1.0 pv.1.0.1 pv0.1.0 pv.1.0.2 pv0.1.1 trA.0.3
    qkB.1.1 qkC.1.1 pv.1.0.3 trB.1.0.0 tr0.1.2 tr0.1.3 ct0.0.0 trB.1.0.1 trB.1.1.0 trB.1.1.1 qkB.1.2 qkC.1.2
    qkB.1.3 ct0.0.1 qkC.1.3 pv.1.1.0 pv0.1.2 rms pv.1.1.1 trB.1.2.0 pv0.1.3 trB.1.2.1 trB.1.3.0 trB.1.3.1
    wo.0 ct.1.0 pv.1.1.2 ct0.1.1 pv.1.1.3 norm.0 proj.1.0 ct0.1.0 ct.1.1 stat.2.0 turn.0 norm.2.0 proj.1.1
    stat.2.1 norm.2.1 wo.1 turn.2.0 turn.2.1 q1.2 qk2.0.0 qk2.0.1 tr2.0.0 qk2.0.2 tr2.0.1 qk2.0.3 q0.0
    pv.2.0.0 pv.2.0.1 tr2.0.2 tr2.0.3 qk2.1.0 qk2.1.1 pv.2.0.2 q0.1 pv.2.0.3 tr2.1.0 tr2.1.1 qk2.1.2 q0.3
    qk2.1.3 pv.2.1.0 pv.2.1.1 tr2.1.2 tr2.1.3 q0.2 pv.2.1.2 pv.2.1.3 ct.2.0 cv ct.2.1 proj.2.0 ck ctx
    stat.3.0 proj.2.1 stat.3.1 norm.3.0 v0.0 norm.3.1 k0.0 turn.3.0 turn.3.1 qk0.0.0 h.2 v0.1 qk0.0.1
    stat.1.0 k0.1 h.1 tr0.0.0 tr0.0.1 h.0 qk0.0.2 qk0.0.3 h.3 norm.1.0 pv0.0.0 pv0.0.1 stat.1.1 tr0.0.2
    tr0.0.3 norm.1.1 f2.0 pv0.0.2 pv0.0.3 f2.1
""")

STAGE1 = {"q1", "k1", "v1", "qkA", "qkB", "qkC", "trA", "trB", "pv", "ct", "proj", "qk2", "tr2", "h", "f2"}
AHEAD = {"rms", "q0", "ctx", "k0", "v0"}


def stage_of(step):
    name = step[0]
    if name in AHEAD or step in (("norm", 0), ("turn", 0)) or name in ("qk0", "tr0", "pv0") and step[1] == 0:
        return 2
    return int(name in STAGE1 or name == "turn" or name in ("stat", "norm") and step[1] > 1)


def slot_uses(order):
    total = {r: sum(USES[step[0]].get(r, 0) for step in order) for r in RINGS}
    return {r: [(total[r] - s + n - 1) // n for s in range(n)] for r, n in RINGS.items()}


class Counts:

    def __init__(self, before, per_turn, turn):
        self.before, self.per_turn, self.turn = before, per_turn, turn
        self.at = {r: 0 for r in RINGS}
        self.of = {}

    def next(self, step):
        taken = {"place": len(self.of)}
        for ring, uses in USES[step[0]].items():
            taken[ring] = []
            for _ in range(uses):
                k, n = self.at[ring], RINGS[ring]
                self.at[ring] += 1
                value = self.before[ring][k % n] + k // n + 1
                total = sum(self.before[ring]) + k + 1
                if self.per_turn is not None:
                    value = self.turn * self.per_turn[ring][k % n] + value
                    total = self.turn * sum(self.per_turn[ring]) + total
                taken[ring].append((k % n, value, total))
        self.of[step] = taken
        return taken


def wait(eng, sem, value):
    if not (isinstance(value, int) and value < 1):
        eng.wait_ge(sem, value)


def decoder(nc, x, ctx, w, out):
    NB, T, C = x.shape
    S = ctx.shape[1]
    H = 16
    KT = C // P
    TT = T // P
    D0 = w["wq0"].shape[1] // H
    D1 = C // H
    M0 = H * D0 // P
    MF = w["f1"].shape[1] // P
    assert (T, C, S, D0, D1) == (256, 256, 77, 64, 16)

    def part(*stages):
        return [step for step in LOOP_ORDER if stage_of(step) in stages]

    parts = [(part(2), 1, (None, None, 0)), (part(0, 2), 1, (0, None, 1)), (LOOP_ORDER, NB - 2, None),
             (part(0, 1), 1, (NB - 1, NB - 2, None)), (part(1), 1, (None, NB - 1, None))]
    before = {r: [0] * n for r, n in RINGS.items()}
    turns = []
    for order, count, batch in parts:
        uses = slot_uses(order)
        turns.append((order, before, uses, count, batch))
        before = {r: [a + count * b for a, b in zip(before[r], uses[r])] for r in RINGS}

    with ExitStack() as stack:
        def sb(name, shape, dt=F32):
            return stack.enter_context(nc.sbuf_tensor(name, shape, dt))

        def sem(name):
            return stack.enter_context(nc.semaphore(name))

        ps = stack.enter_context(nc.psum_tensor("ps", [P, 8, 512], F32))

        split_names = ("wq0", "wv0", "mq", "mk", "mv", "mp", "cq", "cv", "cp", "f1")
        wh, wl = {}, {}
        for n in split_names:
            rows, cols = w[n].shape
            wh[n] = sb("hi_" + n, [P, rows // P, cols], F32R)
            wl[n] = sb("lo_" + n, [P, rows // P, cols], F32R)
        wk0 = sb("wk0", [P, KT, H * D0])
        wo0 = sb("wo0", [P, M0, C])
        wf2 = sb("wf2", [P, MF, C])
        wck = sb("wck", [P, KT, C])
        ident = sb("ident", [P, P])
        identb = sb("identb", [P, P], BF16)
        causal = sb("causal", [P, P], BF16)
        parity = sb("parity", [P, 2])
        minus_half = sb("minus_half", [P, 2])
        gain = sb("gain", [P, 4, KT])
        shift = sb("shift", [P, 3, KT])
        bias = sb("bias", [P, 6, KT])
        bias_h = sb("bias_h", [P, MF])
        qbias = sb("qbias", [P, 2, KT])
        row = sb("row", [P, 3, C])

        xin = sb("xin", [P, TT, C])
        xres = sb("xres", [P, TT, C])
        cin = sb("cin", [P, C])
        stats = sb("stats", [P, 2, TT, 6])
        mv = sb("mv", [P, 2, TT, 2])
        msq = sb("msq", [P, TT])
        veps = sb("veps", [P, 2, TT])
        rstd = sb("rstd", [P, 2, TT])
        xn = sb("xn", [P, TT, C])
        xTh, xTl = sb("xTh", [P, KT, T], F32R), sb("xTl", [P, KT, T], F32R)
        cT = sb("cT", [P, KT, S])
        cTh, cTl = sb("cTh", [P, KT, S], F32R), sb("cTl", [P, KT, S], F32R)
        q0T = sb("q0T", [P, M0, T])
        k0bd = sb("k0bd", [P, M0, 2, S])
        v0p = sb("v0p", [P, 3, H, D0 + 1], BF16)
        vrest = sb("vrest", [P, 512])
        ctxo = sb("ctxo", [P, TT, H * D0])
        coT = sb("coT", [P, M0, T])
        kcbd = sb("kcbd", [P, KT, 2, S])
        vcp = sb("vcp", [P, H, 3, D1 + 1], BF16)
        x1 = sb("x1", [P, TT, C])
        xr1, xr = sb("xr1", [P, TT, C]), sb("xr", [P, TT, C])
        xs = sb("xs", [P, TT, C])
        z = sb("z", [P, TT, C])
        zTh, zTl = sb("zTh", [P, KT, T], F32R), sb("zTl", [P, KT, T], F32R)
        q1T = sb("q1T", [P, KT, T])
        k1bd = sb("k1bd", [P, KT, 2, T])
        v1p = sb("v1p", [P, TT, H, 3, D1 + 1], BF16)
        a = z
        hT = coT
        y = xr
        negmax = sb("negmax", [P, RINGS["bank"], 4])
        probs = [sb("probs0", [P, RINGS["probs0"], 4, S]), sb("probs1", [P, RINGS["probs1"], 4, T])]
        pTh = [sb(f"pTh{i}", [P, RINGS[f"probsT{i}"], 4, P], F16) for i in range(2)]
        pTl = [sb(f"pTl{i}", [P, RINGS[f"probsT{i}"], 4, P], F16) for i in range(2)]
        osum = sb("osum", [P, RINGS["bank"], 4, D1 + 1])
        rsum = sb("rsum", [P, RINGS["bank"], 4])

        stage_w = [probs[1][:, :, :, :].rearrange("p a b c -> p (a b c)"), ctxo[:, :, :].rearrange("p a b -> p (a b)")]

        full = [sem(f"full{i}") for i in range(RINGS["bank"])]
        free = [sem(f"free{i}") for i in range(RINGS["bank"])]
        maxed = sem("maxed")
        hi_done = sem("hi_done")
        vhi_done = sem("vhi_done")
        vmid_done = sem("vmid_done")
        v_done = sem("v_done")
        aggregating, copying = sem("aggregating"), sem("copying")
        chain = sem("chain")
        x_in, xres_in, c_in = sem("x_in"), sem("xres_in"), sem("c_in")
        xres_used, c_used = sem("xres_used"), sem("c_used")
        stat_ready = [sem("stat_ready0"), sem("stat_ready1")]
        rstd_ready = [sem("rstd_ready0"), sem("rstd_ready1")]
        norm_ready = [sem("norm_ready0"), sem("norm_ready1")]
        xr_ready = sem("xr_ready")
        y_ready, y_stored = sem("y_ready"), sem("y_stored")
        w_in = [sem("w_in0"), sem("w_in1")]
        w_free = [sem("w_free0"), sem("w_free1")]
        w_hi, w_bias = sem("w_hi"), sem("w_bias")
        consts_in, consts_made, consts_ready = sem("consts_in"), sem("consts_made"), sem("consts_ready")
        bias_products, bias_read, setup_step = sem("bias_products"), sem("bias_read"), sem("setup_step")

        def bank(s):
            return ps[:, s, :]

        x_v = x.rearrange("b (t p) c -> b p t c", p=P)
        out_v = out.rearrange("b (t p) c -> b p t c", p=P)

        WEIGHTS = [("wq0", 0, None), ("wv0", None, None), ("f1", 3, 2),
                   ("mq", 1, 0), ("mk", 1, 0), ("mv", 1, 0), ("cq", 2, 1), ("cv", None, None),
                   ("mp", None, None), ("cp", None, None)]
        BIAS = {"mq": 0, "mk": 1, "mv": 2, "cq": 3}

        def staged(i):
            rows, cols = w[WEIGHTS[i][0]].shape
            return stage_w[i % 2][:, 0:rows // P * cols].rearrange("p (k n) -> p k n", n=cols)

        def orders(eng, run):
            for order, before, uses, count, batch in turns:
                if batch is not None:
                    run(order, Counts(before, None, 0), batch)
                else:
                    with eng.Fori(0, NB - 2) as i:
                        run(order, Counts(before, uses, i), (i + 1, i, i + 2))

        def value_tiles(step):
            if step[0] == "v0":
                hs = slice(8 * step[1], 8 * step[1] + 8)
                return [v0p[0:S, i, hs, 0:D0] for i in range(3)], vrest[0:S, :].rearrange("p (h d) -> p h d", d=D0)
            if step[0] == "cv":
                return [vcp[0:S, :, i, 0:D1] for i in range(3)], vrest[0:S, 0:C].rearrange("p (h d) -> p h d", d=D1)
            return ([v1p[:, :, :, i, 0:D1].rearrange("p t h d -> p (t h) d") for i in range(3)],
                    vrest[:, :].rearrange("p (h d) -> p h d", d=D1))

        def value_bank(step, s):
            rows, cols, d = {"v0": (S, 512, D0), "cv": (S, C, D1), "v1": (P, 2 * C, D1)}[step[0]]
            return bank(s)[0:rows, 0:cols].rearrange("p (h d) -> p h d", d=d)

        def split_tile(step):
            if step[0] == "ctx":
                return cTh[:], cTl[:], KT, S
            if step == ("turn", 0):
                return xTh[:], xTl[:], KT, T
            ts = slice(step[2] * P, step[2] * P + P)
            return zTh[:, :, ts], zTl[:, :, ts], KT, P

        block = stack.enter_context(nc.Block())

        @block.sync
        def _(sp):
            small = [(gain, "gains"), (shift, "shifts"), (bias, "biases"), (bias_h, "f1b"), (wk0, "wk0"),
                     (wck, "ck"), (wo0, "wo0"), (wf2, "f2")]
            for tile, n in small:
                src = w[n]
                if n in ("wk0", "ck", "wo0", "f2"):
                    src = src.rearrange("(k p) n -> p k n", p=P)
                sp.dma_start(tile[:], src).then_inc(consts_in, 16)
            sp.dma_start(row[:, :, :], w["rows"].unsqueeze(0).to_broadcast([P, 3, C])).then_inc(consts_in, 16)
            for i, (n, _g, _s) in enumerate(WEIGHTS):
                if i >= 2:
                    sp.wait_ge(w_free[i % 2], i // 2)
                    sp.wait_ge(w_bias, i - 1)
                sp.dma_start(staged(i), w[n].rearrange("(k p) n -> p k n", p=P)).then_inc(w_in[i % 2], 16)
            sp.dma_start(xin[:], x_v[0]).then_inc(x_in, 16)
            sp.dma_start(xres[:], x_v[0]).then_inc(xres_in, 16)
            sp.dma_start(cin[0:S, :], ctx[0]).then_inc(c_in, 16)
            sp.wait_ge(c_used, 1)
            sp.dma_start(cin[0:S, :], ctx[1]).then_inc(c_in, 16)
            sp.wait_ge(norm_ready[0], 1)
            sp.dma_start(xin[:], x_v[1]).then_inc(x_in, 16)
            sp.wait_ge(xres_used, 1)
            sp.dma_start(xres[:], x_v[1]).then_inc(xres_in, 16)
            with sp.Fori(2, NB) as b:
                sp.wait_ge(c_used, b)
                sp.dma_start(cin[0:S, :], ctx[bass.ds(b, 1)].rearrange("a s c -> (a s) c")).then_inc(c_in, 16)
                sp.wait_ge(norm_ready[0], b)
                sp.dma_start(xin[:], x_v[bass.ds(b, 1)].rearrange("a p t c -> (a p) t c")).then_inc(x_in, 16)
                sp.wait_ge(xres_used, b)
                sp.dma_start(xres[:], x_v[bass.ds(b, 1)].rearrange("a p t c -> (a p) t c")).then_inc(xres_in, 16)
                sp.wait_ge(y_ready, b * 2 - 2)
                sp.dma_start(out_v[bass.ds(b - 2, 1)].rearrange("a p t c -> (a p) t c"), y[:]).then_inc(y_stored, 16)
            for b in range(NB - 2, NB):
                sp.wait_ge(y_ready, b * 2 + 2)
                sp.dma_start(out_v[b], y[:]).then_inc(y_stored, 16)
            sp.wait_ge(y_stored, 16 * NB + 16)

        @block.gpsimd
        def _(pool):
            nc.gpsimd.memset(ident[:], 0.0).then_inc(consts_made, 1)
            nc.gpsimd.memset(causal[:], 0.0).then_inc(consts_made, 1)
            nc.gpsimd.memset(minus_half[:], -0.5).then_inc(consts_made, 1)
            nc.gpsimd.memset(k0bd[:], 0.0).then_inc(consts_made, 1)
            pool.wait_ge(consts_made, 4)
            nc.gpsimd.affine_select(out=ident[:], in_=ident[:], compare_op=ALU.not_equal, fill=1.0, base=0,
                                    pattern=[[-1, P]], channel_multiplier=1).then_inc(consts_made, 1)
            nc.gpsimd.affine_select(out=causal[:], in_=causal[:], compare_op=ALU.is_ge, fill=MASKED, base=0,
                                    pattern=[[-1, P]], channel_multiplier=1).then_inc(consts_made, 1)
            for part in (v0p, v1p, vcp):
                nc.gpsimd.memset(part[:], 0.0).then_inc(consts_made, 1)
            pool.wait_ge(consts_made, 9)
            nc.gpsimd.memset(v0p[:, 0, :, D0:D0 + 1], 1.0).then_inc(consts_made, 1)
            nc.gpsimd.memset(v1p[:, :, :, 0, D1:D1 + 1], 1.0).then_inc(consts_made, 1)
            nc.gpsimd.memset(vcp[:, :, 0, D1:D1 + 1], 1.0).then_inc(consts_made, 1)
            nc.gpsimd.tensor_copy(identb[:], ident[:]).then_inc(consts_made, 1)

            def inverse_root(stage, ready, ts):
                pool.wait_ge(stat_ready[stage], ready)
                nc.gpsimd.tensor_tensor(rstd[:, stage, ts], veps[:, stage, ts], minus_half[:, ts],
                                        ALU.pow).then_inc(rstd_ready[stage], 1)

            def value_tail(dst, rest, u):
                (s, v, _), (_, _, n) = u["bank"][0], u["vsplit"][0]
                pool.wait_ge(free[s], v)
                pool.sem_inc(copying, 1)
                nc.gpsimd.tensor_copy(dst[1], rest).then_inc(vmid_done, 1)
                pool.wait_ge(vmid_done, n)
                nc.gpsimd.tensor_tensor(dst[2], rest, dst[1], ALU.subtract).then_inc(v_done, 1)

            def run(order, c, batch):
                for step in order:
                    b, u, n = batch[stage_of(step)], c.next(step), step[0]
                    if n == "rms":
                        inverse_root(0, b + 1, slice(0, TT))
                    elif n == "stat":
                        k, t = step[1:]
                        inverse_root(1, b * 6 + 2 * k + t - 1, slice(t, t + 1))
                        if k == 2 and t == 0:
                            pool.wait_ge(y_stored, b * 16 + 16)
                        nc.gpsimd.tensor_tensor((xr1 if k == 1 else xr)[:, t, :], (x1 if k == 1 else xs)[:, t, :], row[:, k - 1, :],
                                                ALU.add).then_inc(xr_ready, 1)
                    elif n in ("v0", "cv", "v1"):
                        value_tail(*value_tiles(step), u)

            orders(pool, run)

        @block.scalar
        def _(act):
            def copy(o, i):
                return nc.scalar.copy(o, i)

            def high_part(u, j, dst, a, b, rows=P):
                s, v, _ = u["bank"][j]
                act.wait_ge(full[s], v)
                copy(dst, bank(s)[0:rows, 0:a * b].rearrange("p (a b) -> p a b", b=b)).then_inc(hi_done, 1)

            def exps(u, stage, slot, heads, width):
                (p, _, _), = slot[f"probs{stage}"]
                (s, _, _), (_, _, total) = u["bank"][0], u["max"][0]
                act.wait_ge(maxed, total)
                for i, h in enumerate(heads):
                    ins = nc.scalar.activation(probs[stage][:, p, h, 0:width],
                                               bank(s)[:, i * width:(i + 1) * width],
                                               ACT.Exp, bias=negmax[:, s, i:i + 1])
                ins.then_inc(free[s], 1)

            def run(order, c, batch):
                for step in order:
                    b, u, n = batch[stage_of(step)], c.next(step), step[0]
                    if n in ("turn", "ctx", "ct"):
                        hi, _, rows, cols = split_tile(step)
                        high_part(u, 0, hi, rows, cols)
                    elif n == "ct0":
                        t, half = step[1:]
                        (s, v, _), = u["bank"]
                        act.wait_ge(full[s], v)
                        copy(coT[:, 4 * half:4 * half + 4, t * P:(t + 1) * P],
                             bank(s).rearrange("p (a b) -> p a b", b=P)).then_inc(free[s], 1)
                    elif n == "q0":
                        (s, v, _), = u["bank"]
                        act.wait_ge(full[s], v)
                        copy(q0T[:, 2 * step[1]:2 * step[1] + 2, :],
                             bank(s).rearrange("p (a b) -> p a b", b=T)).then_inc(free[s], 1)
                    elif n in ("v0", "cv", "v1"):
                        (s, v, _), = u["bank"]
                        act.wait_ge(full[s], v)
                        copy(value_tiles(step)[0][0], value_bank(step, s)).then_inc(vhi_done, 1)
                    elif n == "qk0":
                        exps(u, 0, u, range(4), S)
                    elif n == "qk2":
                        exps(u, 1, u, range(4), S)
                    elif n == "qkA":
                        exps(u, 1, u, range(4), P)
                    elif n == "qkB":
                        exps(u, 1, u, (0, 1), T)
                    elif n == "qkC":
                        exps(u, 1, c.of[("qkB", *step[1:])], (2, 3), T)
                    elif n in ("tr0", "tr2", "trA", "trB"):
                        stage = int(n != "tr0")
                        ring = f"probsT{stage}"
                        for j, (k, _, _) in enumerate(u[ring]):
                            rows = S if n in ("tr0", "tr2") else P
                            high_part(u, j, pTh[stage][0:rows, k, :, :], 4, P, rows)
                    elif n == "q1":
                        (s, v, _), = u["bank"]
                        act.wait_ge(full[s], v)
                        for m in range(KT):
                            ins = nc.scalar.activation(q1T[:, m, :], bank(s)[:, m * T:(m + 1) * T], ACT.Identity,
                                                       bias=qbias[:, step[1] - 1, m:m + 1], scale=float(D1) ** -0.5)
                        ins.then_inc(free[s], 1)
                    elif n == "h":
                        (s, v, _), = u["bank"]
                        act.wait_ge(full[s], v)
                        for m in range(2):
                            ins = nc.scalar.activation(hT[:, 2 * step[1] + m, :], bank(s)[:, m * T:(m + 1) * T], ACT.Relu,
                                                       bias=bias_h[:, 2 * step[1] + m:2 * step[1] + m + 1])
                        ins.then_inc(free[s], 1)

            act.wait_ge(consts_ready, 1)
            orders(act, run)

        @block.vector
        def _(dve):
            steps = [0]

            def done(ins):
                steps[0] += 1
                ins.then_inc(setup_step, 1)
                dve.wait_ge(setup_step, steps[0])

            dve.wait_ge(consts_in, 16 * 9)
            dve.wait_ge(consts_made, 13)
            evens = ident[:, :].rearrange("p (g e d) -> p e g d", e=2, d=D1)
            for e in range(2):
                done(nc.vector.tensor_reduce(parity[:, e:e + 1], evens[:, e], mybir.AxisListType.XY, ALU.add))
            for i, (n, g, s) in enumerate(WEIGHTS):
                dve.wait_ge(w_in[i % 2], 16 * (i // 2 + 1))
                src = staged(i)
                for k in range(src.shape[1]):
                    if g is None:
                        nc.vector.tensor_copy(wh[n][:, k, :], src[:, k, :]).then_inc(w_hi, 1)
                    else:
                        nc.vector.tensor_scalar(wh[n][:, k, :], src[:, k, :], gain[:, g, k:k + 1], None,
                                                ALU.mult).then_inc(w_hi, 1)
                count = sum(w[m].shape[0] // P for m, _, _ in WEIGHTS[:i + 1])
                dve.wait_ge(w_hi, count)
                for k in range(src.shape[1]):
                    scale = 1.0 if g is None else gain[:, g, k:k + 1]
                    ins = nc.vector.scalar_tensor_tensor(out=wl[n][:, k, :], in0=src[:, k, :], scalar=scale,
                                                         in1=wh[n][:, k, :].bitcast(F32), op0=ALU.mult, op1=ALU.subtract)
                ins.then_inc(w_free[i % 2], 1)
                if s is not None:
                    dve.wait_ge(bias_products, sum(1 for m in WEIGHTS[:i + 1] if m[2] is not None))
                    cols = src.shape[2] // P
                    dst = bias_h[:, :] if n == "f1" else bias[:, BIAS[n], :]
                    done(nc.vector.tensor_tensor(dst, ps[:, 0, 0:cols], dst, ALU.add))
                    dve.sem_inc(bias_read, 1)
                if n == "cv":
                    for e, src_bias in enumerate((2, 5)):
                        for k in range(KT):
                            done(nc.vector.tensor_copy(z[:, e, k * P:(k + 1) * P],
                                                       bias[:, src_bias, k:k + 1].to_broadcast([P, P])))
                    dve.sem_inc(bias_read, 1)
                if n in ("mp", "cp"):
                    e = 0 if n == "mp" else 1
                    dve.wait_ge(bias_products, 6 + e)
                    done(nc.vector.tensor_tensor(row[:, e, :], ps[:, 1 + e, 0:C], row[:, e, :], ALU.add))
            for e, i in enumerate((0, 3)):
                done(nc.vector.tensor_scalar(qbias[:, e, :], bias[:, i, :], float(D1) ** -0.5, None, ALU.mult))
            dve.sem_inc(consts_ready, 3)

            def link(u, j, ins):
                _, v, _ = u["chain"][j]
                ins.then_inc(chain, 1)
                dve.wait_ge(chain, v)

            def statistics(u, src, stage, eps, tiles=range(TT)):
                for t in tiles:
                    ins = nc.vector.bn_stats(stats[:, stage, t, :], src[:, t, :])
                link(u, 0, ins)
                dve.sem_inc(aggregating, 1)
                for t in tiles:
                    ins = nc.vector.bn_aggr(mv[:, stage, t, :], stats[:, stage, t, :])
                link(u, 1, ins)
                ts = slice(tiles[0], tiles[-1] + 1)
                mean, var = mv[:, stage, ts, 0], mv[:, stage, ts, 1]
                if stage == 0:
                    link(u, 2, nc.vector.tensor_tensor(msq[:, :], mean, mean, ALU.mult))
                    ins = nc.vector.scalar_tensor_tensor(out=veps[:, 0, :], in0=msq[:, :], scalar=eps, in1=var,
                                                         op0=ALU.add, op1=ALU.add)
                else:
                    ins = nc.vector.tensor_scalar(veps[:, stage, ts], var, eps, None, ALU.add)
                ins.then_inc(stat_ready[stage], 1)

            def normalise(src, stage, value, dst, tiles=range(TT)):
                dve.wait_ge(rstd_ready[stage], value)
                for t in tiles:
                    if stage == 0:
                        ins = nc.vector.tensor_scalar(dst[:, t, :], src[:, t, :], rstd[:, 0, t:t + 1], None, ALU.mult)
                    else:
                        ins = nc.vector.tensor_scalar(dst[:, t, :], src[:, t, :], mv[:, stage, t, 0:1],
                                                      rstd[:, stage, t:t + 1], ALU.subtract, ALU.mult)
                ins.then_inc(norm_ready[stage], 1)

            def low_part(u, j, hi, lo, a, b, rows=P):
                (s, _, _), (_, _, n) = u["bank"][j], u["split"][j]
                dve.wait_ge(hi_done, n)
                src = bank(s)[0:rows, 0:a * b].rearrange("p (a b) -> p a b", b=b)
                nc.vector.tensor_tensor(lo, src, hi, ALU.subtract).then_inc(free[s], 1)

            def maxima(u, heads, width):
                for s, v, _ in u["bank"]:
                    dve.wait_ge(full[s], v)
                    nc.vector.tensor_reduce(negmax[:, s, 0:heads], bank(s)[:, 0:heads * width]
                                            .rearrange("p (h k) -> p h k", h=heads), AX_X, ALU.max,
                                            negate=True).then_inc(maxed, 1)

            def run(order, c, batch):
                for step in order:
                    b, u, n = batch[stage_of(step)], c.next(step), step[0]
                    if n == "rms":
                        dve.wait_ge(x_in, b * 16 + 16)
                        statistics(u, xin, 0, EPS_RMS)
                    elif n == "stat":
                        k, t = step[1:]
                        (s, v, _), = c.of[("wo", t) if k == 1 else ("proj", k - 1, t)]["bank"]
                        dve.wait_ge(free[s], v)
                        statistics(u, x1 if k == 1 else xs, 1, EPS_LN, range(t, t + 1))
                    elif n == "norm":
                        k = step[1]
                        if k == 0:
                            normalise(xin, 0, b + 1, xn)
                        else:
                            t = step[2]
                            normalise(x1 if k == 1 else xs, 1, b * 6 + 2 * k + t - 1, z, range(t, t + 1))
                    elif n in ("turn", "ct", "ctx"):
                        hi, lo, rows, cols = split_tile(step)
                        if n == "ctx":
                            (s, v, _), = u["bank"]
                            dve.wait_ge(full[s], v)
                            dve.sem_inc(c_used, 1)
                            dve.wait_ge(hi_done, u["split"][0][2])
                            nc.vector.tensor_copy(cT[:], bank(s)[:, 0:KT * S].rearrange("p (k c) -> p k c", k=KT))
                        low_part(u, 0, hi.bitcast(F32), lo, rows, cols)
                    elif n == "k0":
                        (s, v, _), = u["bank"]
                        dve.wait_ge(full[s], v)
                        for e in range(2):
                            ins = nc.vector.tensor_copy(
                                k0bd[e * D0:(e + 1) * D0, 4 * step[1]:4 * step[1] + 4, e, :],
                                bank(s)[e * D0:(e + 1) * D0, 0:4 * S].rearrange("p (m k) -> p m k", m=4))
                        ins.then_inc(free[s], 1)
                    elif n in ("v0", "cv", "v1"):
                        (s, v, _), (_, _, total) = u["bank"][0], u["vsplit"][0]
                        parts, rest = value_tiles(step)
                        dve.wait_ge(vhi_done, total)
                        wait(dve, v_done, total - 1)
                        nc.vector.tensor_tensor(rest, value_bank(step, s), parts[0],
                                                ALU.subtract).then_inc(free[s], 1)
                    elif n in ("qk0", "qk2"):
                        maxima(u, 4, S)
                    elif n == "qkA":
                        maxima(u, 4, P)
                    elif n in ("qkB", "qkC"):
                        maxima(u, 2, T)
                    elif n in ("tr0", "tr2", "trA", "trB"):
                        stage = int(n != "tr0")
                        rows = S if n in ("tr0", "tr2") else P
                        for j, (k, _, _) in enumerate(u[f"probsT{stage}"]):
                            low_part(u, j, pTh[stage][0:rows, k], pTl[stage][0:rows, k], 4, P, rows)
                    elif n == "pv0":
                        t, g = step[1:]
                        (s, v, _), = u["bank"]
                        dve.wait_ge(full[s], v)
                        o = bank(s)[:, 0:4 * (D0 + 1)].rearrange("p (h d) -> p h d", h=4)
                        link(u, 0, nc.vector.reciprocal(rsum[:, s, :], o[:, :, D0]))
                        nc.vector.tensor_tensor(
                            ctxo[:, t, 4 * D0 * g:4 * D0 * (g + 1)].rearrange("p (h d) -> p h d", h=4), o[:, :, 0:D0],
                            rsum[:, s, :].unsqueeze(2).to_broadcast([P, 4, D0]), ALU.mult).then_inc(free[s], 1)
                    elif n == "wo":
                        (s, v, _), = u["bank"]
                        t = step[1]
                        dve.wait_ge(full[s], v)
                        dve.wait_ge(xres_in, b * 16 + 16)
                        nc.vector.tensor_tensor(x1[:, t, :], bank(s)[:, 0:C], xres[:, t, :],
                                                ALU.add).then_inc(free[s], 1)
                        if t == 1:
                            dve.wait_ge(free[s], v)
                            dve.sem_inc(xres_used, 1)
                    elif n in ("k1", "ck"):
                        (s, v, _), = u["bank"]
                        dve.wait_ge(full[s], v)
                        width, dst, which = (T, k1bd, 1) if n == "k1" else (S, kcbd, 4)
                        for m in range(KT):
                            for e in range(2):
                                ins = nc.vector.tensor_scalar(dst[:, m, e, :], bank(s)[:, m * width:(m + 1) * width],
                                                              bias[:, which, m:m + 1], parity[:, e:e + 1], ALU.add, ALU.mult)
                        ins.then_inc(free[s], 1)
                    elif n == "pv":
                        _, at, t, r = step
                        (s, v, _), = u["bank"]
                        dve.wait_ge(full[s], v)
                        o = bank(s)[:, 0:4 * 3 * (D1 + 1)].rearrange("p (h i d) -> p h d i", h=4, i=3)
                        link(u, 0, nc.vector.tensor_reduce(osum[:, s], o, AX_X, ALU.add))
                        link(u, 1, nc.vector.reciprocal(rsum[:, s, :], osum[:, s, :, D1]))
                        ins = nc.vector.tensor_tensor(
                            a[:, t, :].rearrange("p (m g e d) -> p g m e d", m=KT, g=4, e=2)[:, r],
                            osum[:, s, :, 0:D1].rearrange("p (m e) d -> p m e d", e=2),
                            rsum[:, s, :].rearrange("p (m e) -> p m e", e=2).unsqueeze(3).to_broadcast([P, KT, 2, D1]),
                            ALU.mult)
                        ins.then_inc(free[s], 1)
                    elif n == "proj":
                        k, t = step[1:]
                        (s, v, _), = u["bank"]
                        dve.wait_ge(full[s], v)
                        dve.wait_ge(xr_ready, b * 6 + 2 * k + t - 1)
                        nc.vector.tensor_tensor(xs[:, t, :], bank(s)[:, 0:C], (xr1 if k == 1 else xr)[:, t, :],
                                                ALU.add).then_inc(free[s], 1)
                    elif n == "f2":
                        (s, v, _), = u["bank"]
                        t = step[1]
                        dve.wait_ge(full[s], v)
                        dve.wait_ge(xr_ready, b * 6 + 5 + t)
                        nc.vector.tensor_tensor(y[:, t, :], bank(s)[:, 0:C], xr[:, t, :],
                                                ALU.add).then_inc(y_ready, 1)
                        dve.wait_ge(y_ready, b * 2 + t + 1)
                        dve.sem_inc(free[s], 1)

            dve.sem_inc(y_stored, 16)
            orders(dve, run)

        @block.tensor
        def _(pe):
            pe.wait_ge(consts_in, 16 * 9)
            products = 0
            for i, (n, g, s) in enumerate(WEIGHTS):
                pe.wait_ge(w_in[i % 2], 16 * (i // 2 + 1))
                src = staged(i)
                if s is not None:
                    if products:
                        pe.wait_ge(bias_read, products)
                    for m in range(src.shape[2] // P):
                        for k in range(KT):
                            ins = pe.matmul(ps[:, 0, m:m + 1], src[:, k, m * P:(m + 1) * P], shift[:, s, k:k + 1],
                                            start=(k == 0), stop=(k == KT - 1))
                    ins.then_inc(bias_products, 1)
                    products += 1
                if n in ("mp", "cp"):
                    e = 0 if n == "mp" else 1
                    pe.wait_ge(bias_read, 6)
                    for k in range(KT):
                        ins = pe.matmul(ps[:, 1 + e, 0:C], z[:, e, k * P:(k + 1) * P], src[:, k, :],
                                        start=(k == 0), stop=(k == KT - 1))
                    ins.then_inc(bias_products, 1)
                pe.drain().then_inc(w_bias, 1)
            pe.wait_ge(consts_ready, 1)

            unread = set()

            def take_bank(u):
                (s, v, _), = u["bank"]
                wait(pe, free[s], v - 1)
                return s

            def landed(c, u, *steps):
                last = {}
                for step in sorted((st for st in steps if st in c.of), key=lambda st: c.of[st]["place"]):
                    s, v, _ = c.of[step]["bank"][0]
                    last[s] = v
                for s, v in last.items():
                    if s not in [x[0] for x in u["bank"]]:
                        pe.wait_ge(free[s], v)

            def three(o, lh, ll, rh, rl, first, last):
                pe.matmul(o, lh, rh, start=first, stop=False)
                pe.matmul(o, lh, rl, start=False, stop=False)
                return pe.matmul(o, ll, rh, start=False, stop=last)

            def turn_tiles(s, src, tiles=range(TT)):
                for k in range(KT):
                    for t in tiles:
                        at = k * len(tiles) + t - tiles[0]
                        ins = pe.transpose(bank(s)[:, at * P:(at + 1) * P],
                                           src[:, t, k * P:(k + 1) * P], ident[:])
                return ins

            def columns_product(u, name, m0, th, tl):
                s = take_bank(u)
                for m in range(2):
                    for k in range(KT):
                        ws = slice((m0 + m) * P, (m0 + m + 1) * P)
                        ins = three(bank(s)[:, m * T:(m + 1) * T], wh[name][:, k, ws], wl[name][:, k, ws],
                                    th[:, k, :], tl[:, k, :], k == 0, k == KT - 1)
                ins.then_inc(full[s], 1)

            def rows_product(u, name, tiles):
                s = take_bank(u)
                for i, t in enumerate(tiles):
                    ts = slice(t * P, (t + 1) * P)
                    for k in range(KT):
                        ins = three(bank(s)[:, i * C:(i + 1) * C], zTh[:, k, ts], zTl[:, k, ts],
                                    wh[name][:, k, :], wl[name][:, k, :], k == 0, k == KT - 1)
                ins.then_inc(full[s], 1)

            def plain_rows_product(u, weight, src, kt, t):
                s = take_bank(u)
                for k in range(kt):
                    ins = pe.matmul(bank(s)[:, 0:C], src[:, k, t * P:(t + 1) * P],
                                    weight[:, k, :], start=(k == 0), stop=(k == kt - 1))
                ins.then_inc(full[s], 1)

            def run(order, c, batch):
                for step in order:
                    b, u, n = batch[stage_of(step)], c.next(step), step[0]
                    if n == "turn":
                        g = step[1]
                        s = take_bank(u)
                        if g == 0:
                            pe.wait_ge(norm_ready[0], b + 1)
                            ins = turn_tiles(s, xn)
                        else:
                            t = step[2]
                            pe.wait_ge(norm_ready[1], b * 6 + 2 * g + t - 1)
                            ins = turn_tiles(s, z, range(t, t + 1))
                        ins.then_inc(full[s], 1)
                    elif n == "ctx":
                        s = take_bank(u)
                        pe.wait_ge(c_in, b * 16 + 16)
                        for k in range(KT):
                            ins = pe.transpose(bank(s)[:, k * S:(k + 1) * S], cin[0:S, k * P:(k + 1) * P],
                                               ident[0:S, 0:S])
                        ins.then_inc(full[s], 1)
                    elif n == "q0":
                        landed(c, u, ("turn", 0))
                        columns_product(u, "wq0", 2 * step[1], xTh, xTl)
                    elif n in ("k0", "ck"):
                        landed(c, u, ("ctx",))
                        s = take_bank(u)
                        ms = range(4 * step[1], 4 * step[1] + 4) if n == "k0" else range(KT)
                        wt = wk0 if n == "k0" else wck
                        for j, m in enumerate(ms):
                            for k in range(KT):
                                ins = pe.matmul(bank(s)[:, j * S:(j + 1) * S], wt[:, k, m * P:(m + 1) * P],
                                                cT[:, k, :], start=(k == 0), stop=(k == KT - 1))
                        ins.then_inc(full[s], 1)
                    elif n in ("v0", "cv"):
                        landed(c, u, ("ctx",))
                        s = take_bank(u)
                        name, cols = ("wv0", slice(512 * step[1], 512 * step[1] + 512)) if n == "v0" else ("cv", slice(0, C))
                        for k in range(KT):
                            ins = three(bank(s)[0:S, 0:cols.stop - cols.start], cTh[:, k, :], cTl[:, k, :],
                                        wh[name][:, k, cols], wl[name][:, k, cols], k == 0, k == KT - 1)
                        ins.then_inc(full[s], 1)
                    elif n == "qk0":
                        t, g = step[1:]
                        s = take_bank(u)
                        if t == 0:
                            landed(c, u, ("q0", g), ("k0", g // 2))
                        for j in range(2):
                            m = 2 * g + j
                            ins = pe.matmul(bank(s)[:, j * 2 * S:(j + 1) * 2 * S], q0T[:, m, t * P:(t + 1) * P],
                                            k0bd[:, m, :, :], start=True, stop=True)
                        ins.then_inc(full[s], 1)
                    elif n == "qk2":
                        t, r = step[1:]
                        s = take_bank(u)
                        if (t, r) == (0, 0):
                            landed(c, u, ("q1", 2))
                        for m in range(KT):
                            ins = pe.matmul(bank(s)[:, m * 2 * S:(m + 1) * 2 * S],
                                            q1T[32 * r:32 * r + 32, m, t * P:(t + 1) * P],
                                            kcbd[32 * r:32 * r + 32, m, :, :], start=True, stop=True)
                        ins.then_inc(full[s], 1)
                    elif n == "qkA":
                        t, r = step[1:]
                        s = take_bank(u)
                        if r == 0:
                            landed(c, u, ("q1", 1), ("k1",))
                        for m in range(KT):
                            pe.matmul(bank(s)[:, m * 2 * P:(m + 1) * 2 * P],
                                      q1T[32 * r:32 * r + 32, m, 0:P], k1bd[32 * r:32 * r + 32, m, :, 0:P],
                                      start=(m == 0), stop=False, skip_group_check=True)
                        pe.matmul(bank(s), identb[:], causal[:].unsqueeze(1).to_broadcast([P, 4, P]),
                                  start=False, stop=True, skip_group_check=True).then_inc(full[s], 1)
                    elif n in ("qkB", "qkC"):
                        t, r = step[1:]
                        m = 0 if n == "qkB" else 1
                        s = take_bank(u)
                        pe.matmul(bank(s), q1T[32 * r:32 * r + 32, m, P:2 * P],
                                  k1bd[32 * r:32 * r + 32, m, :, :], start=True, stop=False,
                                  skip_group_check=True)
                        pe.matmul(bank(s).rearrange("p (e k) -> p e k", e=2)[:, :, P:2 * P], identb[:],
                                  causal[:].unsqueeze(1).to_broadcast([P, 2, P]), start=False, stop=True,
                                  skip_group_check=True).then_inc(full[s], 1)
                    elif n in ("tr0", "tr2", "trA", "trB"):
                        qk = (n.replace("tr", "qk"), *step[1:3])
                        kt = step[3] if n == "trB" else 0
                        if n == "trB":
                            if kt == 0:
                                landed(c, u, qk, ("qkC", *step[1:3]))
                        else:
                            landed(c, u, qk)
                        stage = int(n != "tr0")
                        (p, _, _), = c.of[qk][f"probs{stage}"]
                        rows = S if n in ("tr0", "tr2") else P
                        (slot, _, _), = u[f"probsT{stage}"]
                        assert (stage, slot) not in unread, "turned over probabilities still to be multiplied"
                        unread.add((stage, slot))
                        s = take_bank(u)
                        for h in range(4):
                            ins = pe.transpose(bank(s)[0:rows, h * P:(h + 1) * P],
                                               probs[stage][:, p, h, kt * rows:(kt + 1) * rows], ident[:])
                        ins.then_inc(full[s], 1)
                    elif n == "pv0":
                        t, g = step[1:]
                        if (t, g) == (0, 0):
                            pe.wait_ge(v_done, c.of[("v0", 1)]["vsplit"][0][2])
                        landed(c, u, ("tr0", t, g))
                        (k, _, _), = c.of[("tr0", t, g)]["probsT0"]
                        unread.remove((0, k))
                        s = take_bank(u)
                        for j in range(4):
                            h = 4 * g + j
                            o = bank(s)[:, j * (D0 + 1):(j + 1) * (D0 + 1)]
                            for i in range(3):
                                pe.matmul(o, pTh[0][0:S, k, j, :], v0p[0:S, i, h, :], start=(i == 0), stop=False)
                            for i in range(2):
                                ins = pe.matmul(o, pTl[0][0:S, k, j, :], v0p[0:S, i, h, :], start=False, stop=(i == 1))
                        ins.then_inc(full[s], 1)
                    elif n == "pv":
                        _, at, t, r = step
                        if at == 1 and (t, r) == (0, 0):
                            pe.wait_ge(v_done, c.of[("v1",)]["vsplit"][0][2])
                        trs = [("trB", t, r, kt) for kt in range(2)] if (at, t) == (1, 1) else [("tr2" if at == 2 else "trA", t, r)]
                        landed(c, u, *trs)
                        tiles = [c.of[tr]["probsT1"][0][0] for tr in trs]
                        unread.difference_update((1, k) for k in tiles)
                        s = take_bank(u)
                        o = bank(s)
                        rows = P if at == 1 else S
                        hl, l = 3 * (D1 + 1), 2 * (D1 + 1)
                        for j in range(4):
                            h = j // 2 * 8 + 2 * r + j % 2
                            for kt, k in enumerate(tiles):
                                vp = (v1p[:, kt, h] if at == 1 else vcp[0:S, h]).rearrange("p i d -> p (i d)")
                                pe.matmul(o[:, j * hl:(j + 1) * hl], pTh[1][0:rows, k, j, :], vp, start=(kt == 0),
                                          stop=False, skip_group_check=True)
                                ins = pe.matmul(o[:, j * hl:j * hl + l], pTl[1][0:rows, k, j, :], vp[:, 0:l],
                                                start=False, stop=(kt == len(tiles) - 1), skip_group_check=True)
                        ins.then_inc(full[s], 1)
                    elif n == "ct0":
                        t, half = step[1:]
                        landed(c, u, ("pv0", t, 3))
                        s = take_bank(u)
                        for j in range(4):
                            m = 4 * half + j
                            ins = pe.transpose(bank(s)[:, j * P:(j + 1) * P], ctxo[:, t, m * P:(m + 1) * P], ident[:])
                        ins.then_inc(full[s], 1)
                    elif n == "wo":
                        landed(c, u, ("ct0", step[1], 0), ("ct0", step[1], 1))
                        plain_rows_product(u, wo0, coT, M0, step[1])
                    elif n == "q1":
                        landed(c, u, ("turn", step[1], 0), ("turn", step[1], 1))
                        columns_product(u, "mq" if step[1] == 1 else "cq", 0, zTh, zTl)
                    elif n == "k1":
                        landed(c, u, ("turn", 1, 0), ("turn", 1, 1))
                        columns_product(u, "mk", 0, zTh, zTl)
                    elif n == "v1":
                        landed(c, u, ("turn", 1, 0), ("turn", 1, 1))
                        rows_product(u, "mv", range(TT))
                    elif n == "ct":
                        t = step[2]
                        landed(c, u, ("pv", step[1], t, 3))
                        s = take_bank(u)
                        turn_tiles(s, a, range(t, t + 1)).then_inc(full[s], 1)
                    elif n == "proj":
                        k, t = step[1:]
                        landed(c, u, ("ct", k, t))
                        rows_product(u, "mp" if k == 1 else "cp", range(t, t + 1))
                    elif n == "h":
                        landed(c, u, ("turn", 3, 0), ("turn", 3, 1))
                        columns_product(u, "f1", 2 * step[1], zTh, zTl)
                    elif n == "f2":
                        landed(c, u, *[("h", i) for i in range(4)])
                        plain_rows_product(u, wf2, hT, MF, step[1])

                ahead = [step for step in c.of if stage_of(step) == 2]
                if ahead:
                    landed(c, {"bank": []}, *[st for st in ahead if st[0] in ("q0", "k0", "ctx") or st == ("pv0", 0, 3)])
                    pe.wait_ge(v_done, c.of[("v0", 1)]["vsplit"][0][2])

            orders(pe, run)


def kernel(**inputs):
    import numpy as np
    import concourse.bacc as bacc
    from concourse.bass_utils import run_bass_kernel_spmd

    g = {k.replace("L1_xattn_", "").replace("L0_xattn_", "L0_"): np.asarray(v) for k, v in inputs.items()}
    heads = lambda a: np.ascontiguousarray(a.transpose(1, 0, 2).reshape(a.shape[1], -1))
    cols = lambda *vs: np.ascontiguousarray(
        np.stack([v.reshape(-1, P) for v in vs]).transpose(2, 0, 1))
    arrays = {
        "x": g["x"], "ctx": g["ctx_1024"],
        "wq0": g["L0_wq"], "wk0": g["L0_wk"], "wv0": g["L0_wv"], "wo0": g["L0_wo"],
        "mq": heads(g["mq_w"]), "mk": heads(g["mk_w"]), "mv": heads(g["mv_w"]), "mp": g["m_proj_w"],
        "cq": heads(g["cq_w"]), "ck": heads(g["ck_w"]), "cv": heads(g["cv_w"]), "cp": g["c_proj_w"],
        "f1": g["f_w1"], "f2": g["f_w2"],
        "gains": cols(g["L0_norm_w"], g["ln1_g"], g["ln2_g"], g["ln3_g"]),
        "shifts": cols(g["ln1_b"], g["ln2_b"], g["ln3_b"]),
        "biases": cols(*(g[n].reshape(-1) for n in ("mq_b", "mk_b", "mv_b", "cq_b", "ck_b", "cv_b"))),
        "f1b": np.ascontiguousarray(g["f_b1"].reshape(-1, P).T),
        "rows": np.stack([g["m_proj_b"], g["c_proj_b"], g["f_b2"]]),
    }
    nc = bacc.Bacc("TRN2", target_bir_lowering=False, num_devices=1)
    aps = {}
    arrays = {f"{n}_dram": np.ascontiguousarray(arr) for n, arr in arrays.items()}
    for name, arr in arrays.items():
        aps[name.removesuffix("_dram")] = nc.dram_tensor(name, arr.shape, mybir.dt.from_np(arr.dtype), kind="ExternalInput").ap()
    out = nc.dram_tensor("out", g["x"].shape, F32, kind="ExternalOutput").ap()
    w = {n: ap for n, ap in aps.items() if n not in ("x", "ctx")}
    decoder(nc, aps["x"], aps["ctx"], w, out)
    return run_bass_kernel_spmd(nc, [arrays], core_ids=[0]).results[0]["out"]
```
